# Optimizing a Trainium2 kernel written in Bass

```python
import numpy as np
import jax
import jax.numpy as jnp

def _softmax(x, axis=-1):
    return jax.nn.softmax(x, axis=axis)

def _gelu(x):
    return jax.nn.gelu(x, approximate=True)

def _silu(x):
    return jax.nn.silu(x)

def _sigmoid(x):
    return jax.nn.sigmoid(x)

def _layernorm(x, axis=-1, eps=1e-05):
    m = jnp.mean(x, axis=axis, keepdims=True)
    v = jnp.var(x, axis=axis, keepdims=True)
    return (x - m) / jnp.sqrt(v + eps)

def _scatter_add(tgt, idx, src, axis=0):
    return tgt.at[idx].add(src)

def _segment_sum(src, seg, n):
    return jax.ops.segment_sum(src, seg, n)
kernel_name = 'mk_xattn_seq_d1_seqx_r2_d3dc25'

def setup_inputs(seed: int=0):
    np.random.seed(seed)
    _w = jnp.asarray

    def _rec_inputs():
        import jax
        import jax.numpy as jnp
        _rk = jax.random.key(seed)
        x = -0.0003929 + 0.9999 * jax.random.normal(jax.random.fold_in(_rk, 1), (8, 512, 1024), jnp.float32)
        _lenS = 512 - jax.random.randint(jax.random.fold_in(_rk, 7), (8,), 0, max(1, 512 // 4) + 1, jnp.int32)
        _lenS2 = 512 - jax.random.randint(jax.random.fold_in(_rk, 8), (8,), 0, max(1, 512 // 4) + 1, jnp.int32)
        _ctx_2048P = jax.random.normal(jax.random.fold_in(_rk, 11), (8, 16, 1024), jnp.float32)
        _ctx_2048c = jax.random.dirichlet(jax.random.fold_in(_rk, 511), 0.3 * jnp.ones((16,), jnp.float32), (8, 512))
        _ctx_2048t = jnp.einsum('bsk,bkd->bsd', _ctx_2048c, _ctx_2048P)
        _ctx_2048t = _ctx_2048t * jax.lax.rsqrt(jnp.mean(jnp.square(_ctx_2048t)) + 1e-12) * 0.953939
        ctx_2048 = 2.81802e-05 + 1.00001 * (_ctx_2048t + 0.3 * jax.random.normal(jax.random.fold_in(_rk, 611), (8, 512, 1024), jnp.float32))
        return (x, ctx_2048)
    x, ctx_2048 = _rec_inputs()

    def _L0_xattn_setup():
        import jax, jax.numpy as jnp
        import numpy as np
        B, C1, C2, N = (8, 512, 512, 1024)
        D = C2 // 8
        key = jax.random.key(seed)
        ks = jax.random.split(key, 8)
        s1 = 1.0 / np.sqrt(C1)
        s2 = 1.0 / np.sqrt(C2)
        return {'x1': jax.random.normal(ks[0], (B, C1, N), jnp.float32), 'x2': jax.random.normal(ks[1], (B, C2, N), jnp.float32), 'Wq': jax.random.uniform(ks[2], (D, C1), jnp.float32, -s1, s1), 'bq': jax.random.uniform(ks[3], (D,), jnp.float32, -s1, s1), 'Wk': jax.random.uniform(ks[4], (D, C2), jnp.float32, -s2, s2), 'bk': jax.random.uniform(ks[5], (D,), jnp.float32, -s2, s2), 'Wv': jax.random.uniform(ks[6], (C1, C2), jnp.float32, -s2, s2), 'bv': jax.random.uniform(ks[7], (C1,), jnp.float32, -s2, s2)}
    _L0_xattn_all = _L0_xattn_setup()
    _L0_xattn_in = {k: v for k, v in _L0_xattn_all.items() if k in ('Wq', 'bq', 'Wk', 'bk', 'Wv', 'bv')}
    del _L0_xattn_all
    return {'x': x, 'ctx_2048': ctx_2048, 'L0_xattn_Wq': _L0_xattn_in['Wq'], 'L0_xattn_bq': _L0_xattn_in['bq'], 'L0_xattn_Wk': _L0_xattn_in['Wk'], 'L0_xattn_bk': _L0_xattn_in['bk'], 'L0_xattn_Wv': _L0_xattn_in['Wv'], 'L0_xattn_bv': _L0_xattn_in['bv']}

def reference(x, ctx_2048, L0_xattn_Wq, L0_xattn_bq, L0_xattn_Wk, L0_xattn_bk, L0_xattn_Wv, L0_xattn_bv):
    import jax
    import jax.numpy as jnp

    def _L0_xattn_ref(x1, x2, Wq, bq, Wk, bk, Wv, bv):
        import jax, jax.numpy as jnp
        import numpy as np
        B, C1, C2, N = (8, 512, 512, 1024)
        D = C2 // 8
        q = jnp.einsum('bcn,dc->bnd', x1, Wq) + bq
        k = jnp.einsum('bcn,dc->bdn', x2, Wk) + bk[:, None]
        v = jnp.einsum('bcn,dc->bdn', x2, Wv) + bv[:, None]
        attn = jax.nn.softmax(jnp.einsum('bnd,bdm->bnm', q, k), axis=2)
        attn_out = jnp.einsum('bcm,bnm->bcn', v, attn)
        return attn_out + x1
    x = _L0_xattn_ref(x, ctx_2048, L0_xattn_Wq, L0_xattn_bq, L0_xattn_Wk, L0_xattn_bk, L0_xattn_Wv, L0_xattn_bv)
    return x

_drawn_inputs = setup_inputs


def setup_inputs(seed=0):
    import zlib

    import numpy as np

    out = dict(_drawn_inputs(seed))
    spreads = {}
    factors = {'L0_xattn_bq': 2.746, 'L0_xattn_bk': 8.0}
    for name, (base, spread) in spreads.items():
        noise = np.random.default_rng([zlib.crc32(name.encode()), seed]).standard_normal(out[name].shape)
        drawn = base * np.exp(spread * noise) if base else spread * noise
        out[name] = jnp.asarray(drawn.astype(out[name].dtype))
    for name, factor in factors.items():
        out[name] = (out[name] * factor).astype(out[name].dtype)
    return out
```

```python
from contextlib import ExitStack

import concourse.bass as bass
from concourse import mybir

F32 = mybir.dt.float32
F32R = mybir.dt.float32r
ACT = mybir.ActivationFunctionType
ALU = mybir.AluOpType
AX_X = mybir.AxisListType.X

B, C, N, D = 8, 512, 1024, 64
P = 128
KT = C // P
CT = C // P
MT = N // P
HALVES = 2
NH = N // HALVES
NT = NH // P
ST = HALVES * NT
OG = HALVES * CT
ACC = MT + OG
OUTS = 4
FREE = 2


def build(nc, x1_d, x2_d, wq_d, bq_d, wk_d, bk_d, wv_d, bv_d, out_d):
    with ExitStack() as ctx:
        def sb(name, shape, dt):
            return ctx.enter_context(nc.sbuf_tensor(name, shape, dt))

        def psum(name, shape):
            return ctx.enter_context(nc.psum_tensor(name, shape, F32))

        def sem(name):
            return ctx.enter_context(nc.semaphore(name))

        x1 = sb("x1", [P, 2 * KT * N], F32)
        x2 = sb("x2", [P, 2, N], F32)
        xs_hi = sb("xs_hi", [P, KT, N], F32R)
        xs_lo = sb("xs_lo", [P, KT, N], F32R)
        vt_hi = sb("vt_hi", [P, MT, C], F32R)
        vt_lo = sb("vt_lo", [P, MT, C], F32R)
        probs = sb("probs", [P, NT, N], F32)
        pt_hi = sb("pt_hi", [P, MT, NH], F32R)
        pt_lo = sb("pt_lo", [P, MT, NH], F32R)
        q_st = sb("q_st", [P, N], F32R)
        k_hh = sb("k_hh", [P, N], F32R)
        k_ll = sb("k_ll", [P, N], F32R)
        cross = sb("cross", [D, N], F32)
        full = sb("full", [D, N], F32)
        o_sb = sb("o_sb", [P, OUTS, NH], F32)
        wv_hi = sb("wv_hi", [P, KT, C], F32R)
        wv_lo = sb("wv_lo", [P, KT, C], F32R)
        wq_s = sb("wq_s", [P, KT, P], F32R)
        wk_s = sb("wk_s", [P, KT, P], F32R)
        ident = sb("ident", [P, P], F32)
        bias_q = sb("bias_q", [D, 1], F32)
        bias_k = sb("bias_k", [D, 1], F32)
        bias_v = sb("bias_v", [P, CT], F32)
        negmax = sb("negmax", [P, ST], F32)
        rowsum = sb("rowsum", [P, ST], F32)
        inv = sb("inv", [P, ST], F32)
        wv_raw = probs[:, 0:2, :].rearrange("p a (k c) -> p (a k) c", c=C)
        wq_raw = probs[:, 2, 0:KT * D].rearrange("p (k d) -> p k d", d=D)
        wk_raw = probs[:, 2, KT * D:2 * KT * D].rearrange("p (k d) -> p k d", d=D)
        x0_hi = vt_hi[:].rearrange("p (k a) c -> p k (a c)", k=KT)
        x0_lo = vt_lo[:].rearrange("p (k a) c -> p k (a c)", k=KT)

        acc_ps = psum("acc_ps", [P, 2, NH])
        s_ps = psum("s_ps", [P, 2, 2, NH])
        t_ps = psum("t_ps", [P, 2, NH])

        s_w = sem("s_w")
        s_wv = sem("s_wv")
        s_x1 = [sem(f"s_x1_{k}") for k in range(KT)]
        s_x2 = [sem(f"s_x2_{i}") for i in range(2)]
        s_out = [sem(f"s_out_{i}") for i in range(OUTS)]
        s_id0 = sem("s_id0")
        s_id = sem("s_id")
        s_whi = sem("s_whi")
        s_wlo = sem("s_wlo")
        s_x0hi = sem("s_x0hi")
        s_x0lo = sem("s_x0lo")
        s_xhi = sem("s_xhi")
        s_xlo = sem("s_xlo")
        s_q = sem("s_q")
        s_k = sem("s_k")
        s_cross = sem("s_cross")
        s_qsum = sem("s_qsum")
        s_ksum = sem("s_ksum")
        s_qhi = sem("s_qhi")
        s_qlo = sem("s_qlo")
        s_khi = sem("s_khi")
        s_klo = sem("s_klo")
        s_s = sem("s_s")
        s_max = sem("s_max")
        s_exp = sem("s_exp")
        s_inv = sem("s_inv")
        s_norm = sem("s_norm")
        s_t = sem("s_t")
        s_thi = sem("s_thi")
        s_tlo = sem("s_tlo")
        s_v = sem("s_v")
        s_vhi = sem("s_vhi")
        s_o = sem("s_o")
        s_acc = sem("s_acc")

        block = ctx.enter_context(nc.Block())

        def x1_tile(b, k, lo=0, n=N):
            at = (b % 2) * (KT * N) + (k * N + lo)
            return x1[:, bass.ds(at, n)]

        @block.sync
        def _(sp):
            def load_x2(b, k):
                sp.dma_start(x2[:, k % 2, :], x2_d[b, k * P:(k + 1) * P, :]).then_inc(s_x2[k % 2], 16)

            def store(b, h, c):
                g = h * CT + c
                sp.wait_ge(s_acc, b * ACC + FREE + MT + g + 1)
                sp.dma_start(out_d[b, c * P:(c + 1) * P, h * NH:(h + 1) * NH],
                             o_sb[:, g % OUTS, :]).then_inc(s_out[g % OUTS], 16)

            def batch(b, last):
                if not last:
                    nb = b + 1
                    sp.wait_ge(s_acc, b * ACC + FREE)
                    for k in range(KT):
                        sp.dma_start(x1_tile(nb, k),
                                     x1_d[nb, k * P:(k + 1) * P, :]).then_inc(s_x1[k], 16)
                    for k in range(2):
                        sp.wait_ge(s_xlo, b * 2 * KT + 3 + k)
                        load_x2(nb, k)
                for h in range(HALVES):
                    for c in range(CT):
                        store(b, h, c)
                        if not last and h == 0 and c in (1, 2):
                            sp.wait_ge(s_xlo, b * 2 * KT + 2 * KT + c)
                            load_x2(nb, 1 + c)

            for k in range(2):
                sp.dma_start(x1_tile(0, k), x1_d[0, k * P:(k + 1) * P, :]).then_inc(s_x1[k], 16)
            sp.dma_start(wq_raw, wq_d.rearrange("(k p) d -> p k d", p=P)).then_inc(s_w, 16)
            sp.dma_start(wk_raw, wk_d.rearrange("(k p) d -> p k d", p=P)).then_inc(s_w, 16)
            sp.dma_start(bias_q[:], bq_d.rearrange("(d a) -> d a", a=1)).then_inc(s_w, 16)
            sp.dma_start(bias_k[:], bk_d.rearrange("(d a) -> d a", a=1)).then_inc(s_w, 16)
            sp.dma_start(bias_v[:], bv_d.rearrange("(p c) -> p c", p=P)).then_inc(s_w, 16)
            for k in range(2, KT):
                sp.dma_start(x1_tile(0, k), x1_d[0, k * P:(k + 1) * P, :]).then_inc(s_x1[k], 16)
            load_x2(0, 0)
            load_x2(0, 1)
            sp.dma_start(wv_raw, wv_d.rearrange("(k p) c -> p k c", p=P)).then_inc(s_wv, 16)
            for k in range(2, KT):
                sp.wait_ge(s_xlo, k - 1)
                load_x2(0, k)
            with sp.Fori(0, B - 1) as b:
                batch(b, False)
            batch(B - 1, True)
            for i in range(OUTS):
                sp.wait_ge(s_out[i], 16 * (B * OG // OUTS + 1))

        @block.gpsimd
        def _(pool):
            nc.gpsimd.memset(ident[:], 0.0).then_inc(s_id0, 1)
            pool.wait_ge(s_id0, 1)
            nc.gpsimd.affine_select(out=ident[:], in_=ident[:], compare_op=ALU.not_equal, fill=1.0, base=0,
                                    pattern=[[-1, P]], channel_multiplier=1).then_inc(s_id, 1)

            def low(k, src):
                nc.gpsimd.tensor_tensor(xs_lo[:, k, :], src, xs_hi[:, k, :].bitcast(F32),
                                        ALU.subtract).then_inc(s_xlo, 1)

            for k in range(KT):
                pool.wait_ge(s_xhi, k + 1)
                low(k, x2[:, k % 2, :])
            with pool.Fori(0, B - 1) as b:
                done = b * 2 * KT + KT
                for k in range(KT):
                    pool.wait_ge(s_xhi, done + k + 1)
                    low(k, x1_tile(b + 1, k))
                for k in range(KT):
                    pool.wait_ge(s_xhi, done + KT + k + 1)
                    low(k, x2[:, k % 2, :])

        @block.scalar
        def _(act):
            def copy(out, in_):
                return nc.scalar.activation(out, in_, ACT.Copy)

            def round_x2(b, k):
                act.wait_ge(s_x2[k % 2], (b * 2 + k // 2 + 1) * 16)
                copy(xs_hi[:, k, :], x2[:, k % 2, :]).then_inc(s_xhi, 1)

            def cross_rows(slot):
                copy(cross[:], s_ps[D:2 * D, slot, :, :].rearrange("p a n -> p (a n)")).then_inc(s_cross, 1)

            def q_post(b, slot):
                act.wait_ge(s_q, b + 1)
                cross_rows(slot)
                act.wait_ge(s_qsum, b + 1)
                copy(q_st[0:D, :], full[:]).then_inc(s_qhi, 1)

            def k_post(b, slot):
                act.wait_ge(s_k, b + 1)
                act.wait_ge(s_qsum, b + 1)
                cross_rows(slot)
                act.wait_ge(s_ksum, b + 1)
                for half in range(2):
                    copy(k_hh[half * D:(half + 1) * D, :], full[:]).then_inc(s_khi, 1)

            def exp(b, t, slot):
                act.wait_ge(s_max, b * ST + t + 1)
                nc.scalar.activation(probs[:, t % NT, :], s_ps[:, slot, :, :].rearrange("p a n -> p (a n)"),
                                     ACT.Exp, bias=negmax[:, t:t + 1],
                                     accum_out=rowsum[:, t:t + 1]).then_inc(s_exp, 1)

            def v_hi(b, m):
                act.wait_ge(s_v, b * MT + m + 1)
                copy(vt_hi[:, m, :], acc_ps[:, m % 2, :]).then_inc(s_vhi, 1)

            def t_hi(b, h, m):
                act.wait_ge(s_t, b * 2 * MT + h * MT + m + 1)
                copy(pt_hi[:, m, :], t_ps[:, m % 2, :]).then_inc(s_thi, 1)

            def batch(b, last):
                nb = b + 1
                for m in range(MT):
                    v_hi(b, m)
                    if m >= 2:
                        t_hi(b, 0, m - 2)
                t_hi(b, 0, MT - 2)
                t_hi(b, 0, MT - 1)
                for i in range(NT):
                    exp(b, NT + i, i % 2)
                    if not last:
                        act.wait_ge(s_x1[i], (b + 2) * 16)
                        copy(xs_hi[:, i, :], x1_tile(nb, i)).then_inc(s_xhi, 1)
                if not last:
                    q_post(nb, 0)
                    round_x2(nb, 0)
                    round_x2(nb, 1)
                for m in range(MT):
                    t_hi(b, 1, m)
                    if not last and m in (3, 6):
                        round_x2(nb, 2 + (m == 6))
                if not last:
                    k_post(nb, 1)
                    for i in range(NT):
                        exp(nb, i, i % 2)

            act.wait_ge(s_w, 5 * 16)
            copy(wq_s[:, :, 0:D], wq_raw).then_inc(s_whi, 1)
            copy(wk_s[:, :, 0:D], wk_raw).then_inc(s_whi, 1)
            for k in range(KT):
                act.wait_ge(s_x1[k], 16)
                copy(x0_hi[:, k, :], x1_tile(0, k)).then_inc(s_x0hi, 1)
            for k in range(KT):
                round_x2(0, k)
                if k == 1:
                    act.wait_ge(s_wv, 16)
                    copy(wv_hi[:], wv_raw).then_inc(s_whi, 1)
            q_post(0, 0)
            k_post(0, 1)
            act.wait_ge(s_wlo, 3)
            for i in range(NT):
                exp(0, i, i % 2)
            with act.Fori(0, B - 1) as b:
                batch(b, False)
            batch(B - 1, True)

        @block.vector
        def _(dve):
            def sub(out, a, hi):
                return nc.vector.tensor_tensor(out, a, hi.bitcast(F32), ALU.subtract)

            def join(b, nth, bias, slot, done):
                dve.wait_ge(s_cross, b * 2 + nth + 1)
                nc.vector.scalar_tensor_tensor(
                    out=full[:], in0=s_ps[0:D, slot, :, :].rearrange("p a n -> p (a n)"), scalar=bias[:, 0:1],
                    in1=cross[:], op0=ALU.add, op1=ALU.add).then_inc(done, 1)

            def q_post(b, slot):
                join(b, 0, bias_q, slot, s_qsum)
                dve.wait_ge(s_qhi, b + 1)
                sub(q_st[D:2 * D, :], full[:], q_st[0:D, :]).then_inc(s_qlo, 1)

            def k_post(b, slot):
                dve.wait_ge(s_qlo, b + 1)
                join(b, 1, bias_k, slot, s_ksum)
                for half in range(2):
                    dve.wait_ge(s_khi, b * 2 + half + 1)
                    sub(k_ll[half * D:(half + 1) * D, :], full[:], k_hh[0:D, :]).then_inc(s_klo, 1)

            def neg_max(b, t, slot):
                dve.wait_ge(s_s, b * ST + t + 1)
                nc.vector.tensor_reduce(negmax[:, t:t + 1], s_ps[:, slot, :, :].rearrange("p a n -> p (a n)"),
                                        AX_X, ALU.max, negate=True).then_inc(s_max, 1)

            def normalise(b, t):
                dve.wait_ge(s_exp, b * ST + t + 1)
                nc.vector.reciprocal(inv[:, t:t + 1], rowsum[:, t:t + 1]).then_inc(s_inv, 1)
                dve.wait_ge(s_inv, b * ST + t + 1)
                nc.vector.tensor_scalar(probs[:, t % NT, :], probs[:, t % NT, :], inv[:, t:t + 1], None,
                                        ALU.mult).then_inc(s_norm, 1)

            def v_lo(b, m):
                dve.wait_ge(s_vhi, b * MT + m + 1)
                sub(vt_lo[:, m, :], acc_ps[:, m % 2, :], vt_hi[:, m, :]).then_inc(s_acc, 1)

            def t_lo(b, h, m):
                dve.wait_ge(s_thi, b * 2 * MT + h * MT + m + 1)
                sub(pt_lo[:, m, :], t_ps[:, m % 2, :], pt_hi[:, m, :]).then_inc(s_tlo, 1)

            def out(b, h, c):
                g = h * CT + c
                dve.wait_ge(s_o, b * OG + g + 1)
                dve.wait_ge(s_out[g % OUTS], (b * HALVES + h + 1) * 16)
                nc.vector.scalar_tensor_tensor(
                    out=o_sb[:, g % OUTS, :], in0=acc_ps[:, g % 2, :], scalar=bias_v[:, c:c + 1],
                    in1=x1_tile(b, c, h * NH, NH), op0=ALU.add, op1=ALU.add).then_inc(s_acc, 1)

            def batch(b, last):
                nb = b + 1
                for m in range(MT):
                    v_lo(b, m)
                    if m >= 2:
                        t_lo(b, 0, m - 2)
                t_lo(b, 0, MT - 2)
                t_lo(b, 0, MT - 1)
                neg_max(b, 4, 0)
                neg_max(b, 5, 1)
                normalise(b, 4)
                out(b, 0, 0)
                neg_max(b, 6, 0)
                normalise(b, 5)
                neg_max(b, 7, 1)
                normalise(b, 6)
                out(b, 0, 1)
                normalise(b, 7)
                if not last:
                    q_post(nb, 0)
                out(b, 0, 2)
                for m in range(MT - 1):
                    t_lo(b, 1, m)
                out(b, 0, 3)
                t_lo(b, 1, MT - 1)
                out(b, 1, 0)
                if not last:
                    k_post(nb, 1)
                out(b, 1, 1)
                if not last:
                    neg_max(nb, 0, 0)
                out(b, 1, 2)
                if not last:
                    neg_max(nb, 1, 1)
                    normalise(nb, 0)
                    neg_max(nb, 2, 0)
                    normalise(nb, 1)
                out(b, 1, 3)
                if not last:
                    neg_max(nb, 3, 1)
                    normalise(nb, 2)
                    normalise(nb, 3)

            for i in range(OUTS):
                nc.vector.memset(o_sb[:, i, 0:1], 0.0).then_inc(s_out[i], 16)
            nc.vector.memset(negmax[:], 0.0).then_inc(s_acc, FREE)
            nc.vector.memset(rowsum[:], 0.0).then_inc(s_tlo, FREE)
            dve.wait_ge(s_whi, 1)
            sub(wq_s[:, :, D:2 * D], wq_raw, wq_s[:, :, 0:D]).then_inc(s_wlo, 1)
            dve.wait_ge(s_whi, 2)
            sub(wk_s[:, :, D:2 * D], wk_raw, wk_s[:, :, 0:D]).then_inc(s_wlo, 1)
            for k in range(KT):
                dve.wait_ge(s_x0hi, k + 1)
                sub(x0_lo[:, k, :], x1_tile(0, k), x0_hi[:, k, :]).then_inc(s_x0lo, 1)
            dve.wait_ge(s_whi, 3)
            sub(wv_lo[:], wv_raw, wv_hi[:]).then_inc(s_wlo, 1)
            q_post(0, 0)
            k_post(0, 1)
            neg_max(0, 0, 0)
            neg_max(0, 1, 1)
            normalise(0, 0)
            neg_max(0, 2, 0)
            normalise(0, 1)
            neg_max(0, 3, 1)
            normalise(0, 2)
            normalise(0, 3)
            with dve.Fori(0, B - 1) as b:
                batch(b, False)
            batch(B - 1, True)

        @block.tensor
        def _(pe):
            def project(weights, hi, lo, slot, tiles=None):
                for k in range(KT):
                    if tiles is not None:
                        pe.wait_ge(tiles[0], tiles[1] + k)
                    for part, x in enumerate((hi, lo)):
                        for h in range(HALVES):
                            mm = nc.tensor.matmul(s_ps[:, slot, h, :], weights[:, k, :],
                                                  x[:, k, h * NH:(h + 1) * NH],
                                                  start=(k == 0 and part == 0), stop=(k == KT - 1 and part == 1))
                return mm

            def scores(b, t, slot):
                for h in range(HALVES):
                    cols = slice(h * NH, (h + 1) * NH)
                    nc.tensor.matmul(s_ps[:, slot, h, :], q_st[:, t * P:(t + 1) * P], k_hh[:, cols],
                                     start=True, stop=False)
                    mm = nc.tensor.matmul(s_ps[:, slot, h, :], q_st[:, t * P:(t + 1) * P], k_ll[:, cols],
                                          start=False, stop=True)
                mm.then_inc(s_s, 1)

            def scores_next(b, t):
                if t == 0:
                    pe.wait_ge(s_qsum, b + 1)
                    pe.wait_ge(s_qlo, b + 1)
                    pe.wait_ge(s_klo, b * 2 + 2)
                elif t == 1:
                    pe.wait_ge(s_ksum, b + 1)
                else:
                    pe.wait_ge(s_exp, b * ST + t - 1)
                scores(b, t, t % 2)

            def scores_here(b, t):
                pe.wait_ge(s_exp, b * ST + t - 1)
                scores(b, t, t % 2)

            def turn(b, h, m):
                if m == 0:
                    pe.wait_ge(s_norm, b * ST + (h + 1) * NT)
                pe.wait_ge(s_tlo, b * 2 * MT + h * MT + m + 1)
                for i in range(NT):
                    mm = nc.tensor.transpose(t_ps[:, m % 2, i * P:(i + 1) * P],
                                             probs[:, i, m * P:(m + 1) * P], ident[:])
                mm.then_inc(s_t, 1)

            def v_group(b, m):
                pe.wait_ge(s_acc, b * ACC + m + 1)
                cols = slice(m * P, (m + 1) * P)
                for k in range(KT):
                    for x, w in ((xs_hi, wv_hi), (xs_hi, wv_lo), (xs_lo, wv_hi)):
                        mm = nc.tensor.matmul(acc_ps[:, m % 2, :], x[:, k, cols], w[:, k, :],
                                              start=(k == 0 and w is wv_hi and x is xs_hi),
                                              stop=(k == KT - 1 and x is xs_lo))
                mm.then_inc(s_v, 1)

            def out_part(b, h, c, m):
                g = h * CT + c
                if m == 0:
                    pe.wait_ge(s_acc, b * ACC + MT + g + 1)
                if c == 0:
                    if h == 0 and m == MT - 1:
                        pe.wait_ge(s_acc, b * ACC + FREE + MT)
                    pe.wait_ge(s_tlo, b * 2 * MT + FREE + h * MT + m + 1)
                cols = slice(c * P, (c + 1) * P)
                for v, p in ((vt_hi, pt_hi), (vt_hi, pt_lo), (vt_lo, pt_hi)):
                    mm = nc.tensor.matmul(acc_ps[:, g % 2, :], v[:, m, cols], p[:, m, :],
                                          start=(m == 0 and v is vt_hi and p is pt_hi),
                                          stop=(m == MT - 1 and v is vt_lo))
                if m == MT - 1:
                    mm.then_inc(s_o, 1)

            def q_next(b):
                pe.wait_ge(s_exp, b * ST - 1)
                pe.wait_ge(s_xlo, b * 2 * KT)
                project(wq_s, xs_hi, xs_lo, 0).then_inc(s_q, 1)

            def k_next(b):
                pe.wait_ge(s_exp, b * ST)
                pe.wait_ge(s_xlo, b * 2 * KT + KT)
                project(wk_s, xs_hi, xs_lo, 1).then_inc(s_k, 1)

            def batch(b, last):
                nb = b + 1
                for m in range(MT):
                    v_group(b, m)
                    if m >= 2:
                        turn(b, 0, m - 2)
                turn(b, 0, MT - 2)
                turn(b, 0, MT - 1)
                for c in range(CT):
                    for m in range(MT):
                        if c < 2 and m % 4 == 0:
                            scores_here(b, NT + 2 * c + m // 4)
                        if c == 2 and m == 0 and not last:
                            q_next(nb)
                        out_part(b, 0, c, m)
                        if c == CT - 1:
                            turn(b, 1, m)
                for c in range(CT):
                    for m in range(MT):
                        if not last:
                            if c == 1 and m == 0:
                                k_next(nb)
                            if (c, m) in ((2, 4), (3, 0), (3, 4)):
                                scores_next(nb, 2 * c + m // 4 - 5)
                        out_part(b, 1, c, m)
                if not last:
                    scores_next(nb, 3)

            pe.wait_ge(s_id, 1)
            pe.wait_ge(s_wlo, 1)
            project(wq_s, x0_hi, x0_lo, 0, (s_x0lo, 1)).then_inc(s_q, 1)
            pe.wait_ge(s_wlo, 2)
            project(wk_s, xs_hi, xs_lo, 1, (s_xlo, 1)).then_inc(s_k, 1)
            for t in range(NT):
                scores_next(0, t)
            pe.wait_ge(s_wlo, 3)
            with pe.Fori(0, B - 1) as b:
                batch(b, False)
            batch(B - 1, True)


_INS = ["x", "ctx_2048", "L0_xattn_Wq", "L0_xattn_bq", "L0_xattn_Wk", "L0_xattn_bk", "L0_xattn_Wv", "L0_xattn_bv"]


def kernel(**inputs):
    import numpy as _np
    import concourse.bacc as _bacc
    from concourse import mybir as _mybir
    from concourse.bass_utils import run_bass_kernel_spmd as _run

    nc = _bacc.Bacc("TRN2", target_bir_lowering=False, num_devices=1)
    arrays, args = {}, []
    for name in _INS:
        a = _np.asarray(inputs[name])
        if a.ndim == 2:
            a = a.T
        if name == "L0_xattn_bv":
            a = a.reshape(CT, P).T.reshape(C)
        a = _np.ascontiguousarray(a)
        arrays[f"in_{name}_dram"] = a
        args.append(nc.dram_tensor(f"in_{name}_dram", a.shape, _mybir.dt.from_np(a.dtype), kind="ExternalInput").ap())
    out = nc.dram_tensor("out_dram", (B, C, N), F32, kind="ExternalOutput").ap()
    build(nc, *args, out)
    r = _run(nc, [arrays], core_ids=[0])
    return r.results[0]["out_dram"]
```

```python
from contextlib import ExitStack

import concourse.bass as bass
from concourse import mybir

F32 = mybir.dt.float32
F32R = mybir.dt.float32r
ACT = mybir.ActivationFunctionType
ALU = mybir.AluOpType
AX_X = mybir.AxisListType.X

B, C, N, D = 8, 512, 1024, 64
P = 128
KT = C // P
CT = C // P
MT = N // P
HALVES = 2
NH = N // HALVES
NT = NH // P
ST = HALVES * NT
OG = HALVES * CT
ACC = MT + OG
VT = MT // 2
OUTS = 4
FREE = 2


def build(nc, x1_d, x2_d, wq_d, bq_d, wk_d, bk_d, wv_d, bv_d, out_d):
    with ExitStack() as ctx:
        def sb(name, shape, dt):
            return ctx.enter_context(nc.sbuf_tensor(name, shape, dt))

        def psum(name, shape):
            return ctx.enter_context(nc.psum_tensor(name, shape, F32))

        def sem(name):
            return ctx.enter_context(nc.semaphore(name))

        x1 = sb("x1", [P, 2 * KT * N], F32)
        x2 = sb("x2", [P, 2, N], F32)
        xs_hi = sb("xs_hi", [P, KT, N], F32R)
        xs_lo = sb("xs_lo", [P, KT, N], F32R)
        vt_hi = sb("vt_hi", [P, MT, C], F32R)
        vt_lo = sb("vt_lo", [P, MT, C], F32R)
        probs = sb("probs", [P, NT, N], F32)
        pt_hi = sb("pt_hi", [P, MT, NH], F32R)
        pt_lo = sb("pt_lo", [P, MT, NH], F32R)
        q_st = sb("q_st", [P, N], F32R)
        k_hh = sb("k_hh", [P, N], F32R)
        k_ll = sb("k_ll", [P, N], F32R)
        cross = sb("cross", [D, N], F32)
        full = sb("full", [D, N], F32)
        o_sb = sb("o_sb", [P, OUTS, NH], F32)
        wv_hi = sb("wv_hi", [P, KT, C], F32R)
        wv_lo = sb("wv_lo", [P, KT, C], F32R)
        wq_s = sb("wq_s", [P, KT, P], F32R)
        wk_s = sb("wk_s", [P, KT, P], F32R)
        ident = sb("ident", [P, P], F32)
        bias_q = sb("bias_q", [D, 1], F32)
        bias_k = sb("bias_k", [D, 1], F32)
        bias_v = sb("bias_v", [P, CT], F32)
        negmax = sb("negmax", [P, ST], F32)
        rowsum = sb("rowsum", [P, ST], F32)
        inv = sb("inv", [P, ST], F32)
        wv_raw = probs[:, 0:2, :].rearrange("p a (k c) -> p (a k) c", c=C)
        wq_raw = probs[:, 2, 0:KT * D].rearrange("p (k d) -> p k d", d=D)
        wk_raw = probs[:, 2, KT * D:2 * KT * D].rearrange("p (k d) -> p k d", d=D)
        x0_hi = pt_hi[:].rearrange("p (k a) n -> p k (a n)", k=KT)
        x0_lo = pt_lo[:].rearrange("p (k a) n -> p k (a n)", k=KT)

        acc_ps = psum("acc_ps", [P, 2, NH])
        s_ps = psum("s_ps", [P, 2, 2, NH])
        t_ps = psum("t_ps", [P, 2, NH])

        s_wk = sem("s_wk")
        s_wq = sem("s_wq")
        s_bk = sem("s_bk")
        s_bqv = sem("s_bqv")
        s_wv = [sem(f"s_wv_{k}") for k in range(KT)]
        s_x20 = [sem(f"s_x20_{k}") for k in range(KT)]
        s_x1 = [sem(f"s_x1_{k}") for k in range(KT)]
        s_x2 = [sem(f"s_x2_{i}") for i in range(2)]
        s_out = [sem(f"s_out_{i}") for i in range(OUTS)]
        s_id0 = sem("s_id0")
        s_id = sem("s_id")
        s_wkhi = sem("s_wkhi")
        s_wklo = sem("s_wklo")
        s_wqhi = sem("s_wqhi")
        s_wqlo = sem("s_wqlo")
        s_wvhi = sem("s_wvhi")
        s_wvlo = sem("s_wvlo")
        s_x1hi = sem("s_x1hi")
        s_x1lo_e = sem("s_x1lo_e")
        s_x1lo_o = sem("s_x1lo_o")
        s_x2hi = sem("s_x2hi")
        s_x2lo = sem("s_x2lo")
        s_q = sem("s_q")
        s_k = sem("s_k")
        s_qcross = sem("s_qcross")
        s_kcross = sem("s_kcross")
        s_qsum = sem("s_qsum")
        s_ksum = sem("s_ksum")
        s_qhi = sem("s_qhi")
        s_qlo = sem("s_qlo")
        s_khi = sem("s_khi")
        s_klo = sem("s_klo")
        s_s = sem("s_s")
        s_max = sem("s_max")
        s_exp = sem("s_exp")
        s_inv = sem("s_inv")
        s_norm = sem("s_norm")
        s_t = sem("s_t")
        s_thi = sem("s_thi")
        s_tlo = sem("s_tlo")
        s_v = sem("s_v")
        s_vhi = sem("s_vhi")
        s_o = sem("s_o")
        s_acc = sem("s_acc")

        block = ctx.enter_context(nc.Block())

        def x1_tile(b, k, lo=0, n=N):
            at = (b % 2) * (KT * N) + (k * N + lo)
            return x1[:, bass.ds(at, n)]

        def x2_raw0(k):
            return x1_tile(1, k)

        @block.sync
        def _(sp):
            def load_x2(b, k):
                sp.dma_start(x2[:, k % 2, :], x2_d[b, k * P:(k + 1) * P, :]).then_inc(s_x2[k % 2], 16)

            def store(b, h, c):
                g = h * CT + c
                sp.wait_ge(s_acc, b * ACC + FREE + MT + g + 1)
                sp.dma_start(out_d[b, c * P:(c + 1) * P, h * NH:(h + 1) * NH],
                             o_sb[:, g % OUTS, :]).then_inc(s_out[g % OUTS], 16)

            def batch(b, last):
                if not last:
                    nb = b + 1
                    sp.wait_ge(s_acc, b * ACC + FREE)
                    sp.wait_ge(s_x1hi, b * KT + KT)
                    sp.wait_ge(s_x2lo, b * KT + KT)
                    for k in range(KT):
                        sp.dma_start(x1_tile(nb, k),
                                     x1_d[nb, k * P:(k + 1) * P, :]).then_inc(s_x1[k], 16)
                    for k in range(2):
                        load_x2(nb, k)
                for h in range(HALVES):
                    for c in range(CT):
                        store(b, h, c)
                        if not last and h == 0 and c in (1, 2):
                            sp.wait_ge(s_x2lo, b * KT + KT + c)
                            load_x2(nb, 1 + c)

            for k in range(KT):
                rows = slice(k * P, (k + 1) * P)
                sp.dma_start(x2_raw0(k), x2_d[0, rows, :]).then_inc(s_x20[k], 16)
                if k == 0:
                    sp.dma_start(wk_raw, wk_d.rearrange("(k p) d -> p k d", p=P)).then_inc(s_wk, 16)
                sp.dma_start(wv_raw[:, k, :], wv_d[rows, :]).then_inc(s_wv[k], 16)
            sp.dma_start(bias_k[:], bk_d.rearrange("(d a) -> d a", a=1)).then_inc(s_bk, 16)
            for k in range(KT):
                sp.dma_start(x1_tile(0, k), x1_d[0, k * P:(k + 1) * P, :]).then_inc(s_x1[k], 16)
                if k == 0:
                    sp.dma_start(wq_raw, wq_d.rearrange("(k p) d -> p k d", p=P)).then_inc(s_wq, 16)
                    sp.dma_start(bias_q[:], bq_d.rearrange("(d a) -> d a", a=1)).then_inc(s_bqv, 16)
                    sp.dma_start(bias_v[:], bv_d.rearrange("(p c) -> p c", p=P)).then_inc(s_bqv, 16)
            with sp.Fori(0, B - 1) as b:
                batch(b, False)
            batch(B - 1, True)
            for i in range(OUTS):
                sp.wait_ge(s_out[i], 16 * (B * OG // OUTS + 1))

        @block.gpsimd
        def _(pool):
            def low(out, src, hi):
                return nc.gpsimd.tensor_tensor(out, src, hi.bitcast(F32), ALU.subtract)

            nc.gpsimd.memset(ident[:], 0.0).then_inc(s_id0, 1)
            pool.wait_ge(s_id0, 1)
            nc.gpsimd.affine_select(out=ident[:], in_=ident[:], compare_op=ALU.not_equal, fill=1.0, base=0,
                                    pattern=[[-1, P]], channel_multiplier=1).then_inc(s_id, 1)
            for k in (0, 2):
                pool.wait_ge(s_x1hi, k + 1)
                low(x0_lo[:, k, :], x1_tile(0, k), x0_hi[:, k, :]).then_inc(s_x1lo_e, 1)
            with pool.Fori(0, B - 1) as b:
                for k in (0, 2):
                    pool.wait_ge(s_x1hi, b * KT + KT + k + 1)
                    low(xs_lo[:, k, :], x1_tile(b + 1, k), xs_hi[:, k, :]).then_inc(s_x1lo_e, 1)
                for k in range(KT):
                    pool.wait_ge(s_x2hi, b * KT + KT + k + 1)
                    low(xs_lo[:, k, :], x2[:, k % 2, :], xs_hi[:, k, :]).then_inc(s_x2lo, 1)

        @block.scalar
        def _(act):
            def copy(out, in_):
                return nc.scalar.activation(out, in_, ACT.Copy)

            def round_x1(b, k):
                act.wait_ge(s_x1[k], (b + 1) * 16)
                copy(xs_hi[:, k, :], x1_tile(b, k)).then_inc(s_x1hi, 1)

            def round_x2(b, k):
                act.wait_ge(s_x2[k % 2], (b * 2 + k // 2 - 1) * 16)
                copy(xs_hi[:, k, :], x2[:, k % 2, :]).then_inc(s_x2hi, 1)

            def cross_rows(slot):
                return copy(cross[:], s_ps[D:2 * D, slot, :, :].rearrange("p a n -> p (a n)"))

            def q_post(b):
                act.wait_ge(s_q, b + 1)
                cross_rows(0).then_inc(s_qcross, 1)
                act.wait_ge(s_qsum, b + 1)
                copy(q_st[0:D, :], full[:]).then_inc(s_qhi, 1)

            def k_cross(b):
                act.wait_ge(s_k, b + 1)
                cross_rows(1).then_inc(s_kcross, 1)

            def k_high(b):
                act.wait_ge(s_ksum, b + 1)
                for half in range(2):
                    copy(k_hh[half * D:(half + 1) * D, :], full[:]).then_inc(s_khi, 1)

            def exp(b, t):
                act.wait_ge(s_max, b * ST + t + 1)
                nc.scalar.activation(probs[:, t % NT, :], s_ps[:, t % 2, :, :].rearrange("p a n -> p (a n)"),
                                     ACT.Exp, bias=negmax[:, t:t + 1],
                                     accum_out=rowsum[:, t:t + 1]).then_inc(s_exp, 1)

            def v_hi(b, m):
                act.wait_ge(s_v, b * MT + m + 1)
                copy(vt_hi[:, m, :], acc_ps[:, m % 2, :]).then_inc(s_vhi, 1)

            def t_hi(b, h, m):
                act.wait_ge(s_t, b * 2 * MT + h * MT + m + 1)
                copy(pt_hi[:, m, :], t_ps[:, m % 2, :]).then_inc(s_thi, 1)

            def batch(b, last):
                nb = b + 1
                if not last:
                    round_x1(nb, 0)
                for m in range(VT, MT):
                    t_hi(b, 0, m)
                exp(b, 4)
                if not last:
                    round_x1(nb, 1)
                exp(b, 5)
                if not last:
                    round_x1(nb, 2)
                    round_x1(nb, 3)
                exp(b, 6)
                exp(b, 7)
                if not last:
                    q_post(nb)
                    round_x2(nb, 0)
                    round_x2(nb, 1)
                for m in range(MT):
                    t_hi(b, 1, m)
                    if not last and m == 3:
                        round_x2(nb, 2)
                    if not last and m == 6:
                        round_x2(nb, 3)
                if last:
                    return
                k_cross(nb)
                k_high(nb)
                for t in range(NT):
                    exp(nb, t)
                for m in range(MT):
                    v_hi(nb, m)
                    if m >= MT - VT:
                        t_hi(nb, 0, m - (MT - VT))

            for k in range(KT):
                act.wait_ge(s_x20[k], 16)
                copy(xs_hi[:, k, :], x2_raw0(k)).then_inc(s_x2hi, 1)
                if k == 0:
                    act.wait_ge(s_wk, 16)
                    copy(wk_s[:, :, 0:D], wk_raw).then_inc(s_wkhi, 1)
                act.wait_ge(s_wv[k], 16)
                copy(wv_hi[:, k, :], wv_raw[:, k, :]).then_inc(s_wvhi, 1)

            def round_x0(k):
                act.wait_ge(s_x1[k], 16)
                copy(x0_hi[:, k, :], x1_tile(0, k)).then_inc(s_x1hi, 1)

            act.wait_ge(s_wq, 16)
            copy(wq_s[:, :, 0:D], wq_raw).then_inc(s_wqhi, 1)
            round_x0(0)
            k_cross(0)
            v_hi(0, 0)
            round_x0(1)
            v_hi(0, 1)
            round_x0(2)
            k_high(0)
            round_x0(3)
            v_hi(0, 2)
            q_post(0)
            v_hi(0, 3)
            v_hi(0, 4)
            act.wait_ge(s_wqlo, 1)
            act.wait_ge(s_wklo, 1)
            act.wait_ge(s_wvlo, KT)
            exp(0, 0)
            exp(0, 1)
            v_hi(0, 5)
            exp(0, 2)
            exp(0, 3)
            v_hi(0, 6)
            v_hi(0, 7)
            for m in range(VT):
                t_hi(0, 0, m)
            with act.Fori(0, B - 1) as b:
                batch(b, False)
            batch(B - 1, True)

        @block.vector
        def _(dve):
            def sub(out, a, hi):
                return nc.vector.tensor_tensor(out, a, hi.bitcast(F32), ALU.subtract)

            def join(bias, slot):
                return nc.vector.scalar_tensor_tensor(
                    out=full[:], in0=s_ps[0:D, slot, :, :].rearrange("p a n -> p (a n)"), scalar=bias[:, 0:1],
                    in1=cross[:], op0=ALU.add, op1=ALU.add)

            def q_sum(b):
                dve.wait_ge(s_qcross, b + 1)
                join(bias_q, 0).then_inc(s_qsum, 1)

            def q_low(b):
                dve.wait_ge(s_qhi, b + 1)
                sub(q_st[D:2 * D, :], full[:], q_st[0:D, :]).then_inc(s_qlo, 1)

            def k_sum(b):
                dve.wait_ge(s_kcross, b + 1)
                join(bias_k, 1).then_inc(s_ksum, 1)

            def k_low(b):
                for half in range(2):
                    dve.wait_ge(s_khi, b * 2 + half + 1)
                    sub(k_ll[half * D:(half + 1) * D, :], full[:], k_hh[0:D, :]).then_inc(s_klo, 1)

            def low_x1(b, k):
                dve.wait_ge(s_x1hi, b * KT + k + 1)
                sub(xs_lo[:, k, :], x1_tile(b, k), xs_hi[:, k, :]).then_inc(s_x1lo_o, 1)

            def neg_max(b, t):
                dve.wait_ge(s_s, b * ST + t + 1)
                nc.vector.tensor_reduce(negmax[:, t:t + 1], s_ps[:, t % 2, :, :].rearrange("p a n -> p (a n)"),
                                        AX_X, ALU.max, negate=True).then_inc(s_max, 1)

            def normalise(b, t):
                dve.wait_ge(s_exp, b * ST + t + 1)
                nc.vector.reciprocal(inv[:, t:t + 1], rowsum[:, t:t + 1]).then_inc(s_inv, 1)
                dve.wait_ge(s_inv, b * ST + t + 1)
                nc.vector.tensor_scalar(probs[:, t % NT, :], probs[:, t % NT, :], inv[:, t:t + 1], None,
                                        ALU.mult).then_inc(s_norm, 1)

            def v_lo(b, m):
                dve.wait_ge(s_vhi, b * MT + m + 1)
                sub(vt_lo[:, m, :], acc_ps[:, m % 2, :], vt_hi[:, m, :]).then_inc(s_acc, 1)

            def t_lo(b, h, m):
                dve.wait_ge(s_thi, b * 2 * MT + h * MT + m + 1)
                sub(pt_lo[:, m, :], t_ps[:, m % 2, :], pt_hi[:, m, :]).then_inc(s_tlo, 1)

            def out(b, h, c):
                g = h * CT + c
                dve.wait_ge(s_o, b * OG + g + 1)
                dve.wait_ge(s_out[g % OUTS], (b * HALVES + h + 1) * 16)
                nc.vector.scalar_tensor_tensor(
                    out=o_sb[:, g % OUTS, :], in0=acc_ps[:, g % 2, :], scalar=bias_v[:, c:c + 1],
                    in1=x1_tile(b, c, h * NH, NH), op0=ALU.add, op1=ALU.add).then_inc(s_acc, 1)

            def batch(b, last):
                nb = b + 1
                neg_max(b, 4)
                for m in range(VT, MT):
                    t_lo(b, 0, m)
                neg_max(b, 5)
                normalise(b, 4)
                out(b, 0, 0)
                if not last:
                    low_x1(nb, 1)
                neg_max(b, 6)
                normalise(b, 5)
                if not last:
                    low_x1(nb, 3)
                neg_max(b, 7)
                normalise(b, 6)
                out(b, 0, 1)
                normalise(b, 7)
                if not last:
                    q_sum(nb)
                    q_low(nb)
                out(b, 0, 2)
                for m in range(MT - 1):
                    t_lo(b, 1, m)
                out(b, 0, 3)
                t_lo(b, 1, MT - 1)
                out(b, 1, 0)
                if not last:
                    k_sum(nb)
                    k_low(nb)
                out(b, 1, 1)
                if last:
                    out(b, 1, 2)
                    out(b, 1, 3)
                    return
                neg_max(nb, 0)
                out(b, 1, 2)
                neg_max(nb, 1)
                normalise(nb, 0)
                neg_max(nb, 2)
                normalise(nb, 1)
                out(b, 1, 3)
                neg_max(nb, 3)
                normalise(nb, 2)
                normalise(nb, 3)
                for m in range(MT):
                    v_lo(nb, m)
                    if m >= MT - VT:
                        t_lo(nb, 0, m - (MT - VT))

            for i in range(OUTS):
                nc.vector.memset(o_sb[:, i, 0:1], 0.0).then_inc(s_out[i], 16)
            nc.vector.memset(negmax[:], 0.0).then_inc(s_acc, FREE)
            nc.vector.memset(rowsum[:], 0.0).then_inc(s_tlo, FREE)
            for k in range(KT):
                dve.wait_ge(s_x2hi, k + 1)
                sub(xs_lo[:, k, :], x2_raw0(k), xs_hi[:, k, :]).then_inc(s_x2lo, 1)
                if k == 0:
                    dve.wait_ge(s_wkhi, 1)
                    sub(wk_s[:, :, D:2 * D], wk_raw, wk_s[:, :, 0:D]).then_inc(s_wklo, 1)
                dve.wait_ge(s_wvhi, k + 1)
                sub(wv_lo[:, k, :], wv_raw[:, k, :], wv_hi[:, k, :]).then_inc(s_wvlo, 1)

            def low_x0(k):
                dve.wait_ge(s_x1hi, k + 1)
                sub(x0_lo[:, k, :], x1_tile(0, k), x0_hi[:, k, :]).then_inc(s_x1lo_o, 1)

            dve.wait_ge(s_wqhi, 1)
            sub(wq_s[:, :, D:2 * D], wq_raw, wq_s[:, :, 0:D]).then_inc(s_wqlo, 1)
            dve.wait_ge(s_bk, 16)
            dve.wait_ge(s_bqv, 2 * 16)
            k_sum(0)
            v_lo(0, 0)
            low_x0(1)
            v_lo(0, 1)
            k_low(0)
            low_x0(3)
            v_lo(0, 2)
            q_sum(0)
            q_low(0)
            v_lo(0, 3)
            v_lo(0, 4)
            neg_max(0, 0)
            neg_max(0, 1)
            normalise(0, 0)
            v_lo(0, 5)
            normalise(0, 1)
            neg_max(0, 2)
            neg_max(0, 3)
            normalise(0, 2)
            v_lo(0, 6)
            normalise(0, 3)
            v_lo(0, 7)
            for m in range(VT):
                t_lo(0, 0, m)
            with dve.Fori(0, B - 1) as b:
                batch(b, False)
            batch(B - 1, True)

        @block.tensor
        def _(pe):
            def project_tile(weights, hi, lo, slot, k):
                for part, x in enumerate((hi, lo)):
                    for h in range(HALVES):
                        mm = nc.tensor.matmul(s_ps[:, slot, h, :], weights[:, k, :],
                                              x[:, k, h * NH:(h + 1) * NH],
                                              start=(k == 0 and part == 0), stop=(k == KT - 1 and part == 1))
                return mm

            def scores(t):
                for h in range(HALVES):
                    cols = slice(h * NH, (h + 1) * NH)
                    nc.tensor.matmul(s_ps[:, t % 2, h, :], q_st[:, t * P:(t + 1) * P], k_hh[:, cols],
                                     start=True, stop=False)
                    mm = nc.tensor.matmul(s_ps[:, t % 2, h, :], q_st[:, t * P:(t + 1) * P], k_ll[:, cols],
                                          start=False, stop=True)
                mm.then_inc(s_s, 1)

            def scores_next(b, t):
                if t == 0:
                    pe.wait_ge(s_qsum, b + 1)
                    pe.wait_ge(s_qlo, b + 1)
                    pe.wait_ge(s_klo, b * 2 + 2)
                elif t == 1:
                    pe.wait_ge(s_ksum, b + 1)
                else:
                    pe.wait_ge(s_exp, b * ST + t - 1)
                scores(t)

            def scores_here(b, t):
                pe.wait_ge(s_exp, b * ST + t - 1)
                scores(t)

            def turn(b, h, m):
                if m == 0:
                    pe.wait_ge(s_norm, b * ST + (h + 1) * NT)
                pe.wait_ge(s_tlo, b * 2 * MT + h * MT + m + 1)
                for i in range(NT):
                    mm = nc.tensor.transpose(t_ps[:, m % 2, i * P:(i + 1) * P],
                                             probs[:, i, m * P:(m + 1) * P], ident[:])
                mm.then_inc(s_t, 1)

            def v_tile(m, k):
                cols = slice(m * P, (m + 1) * P)
                for x, w in ((xs_hi, wv_hi), (xs_hi, wv_lo), (xs_lo, wv_hi)):
                    mm = nc.tensor.matmul(acc_ps[:, m % 2, :], x[:, k, cols], w[:, k, :],
                                          start=(k == 0 and w is wv_hi and x is xs_hi),
                                          stop=(k == KT - 1 and x is xs_lo))
                return mm

            def v_group(b, m):
                pe.wait_ge(s_acc, b * ACC + m + 1)
                for k in range(KT):
                    mm = v_tile(m, k)
                mm.then_inc(s_v, 1)

            def out_part(b, h, c, m):
                g = h * CT + c
                if m == 0:
                    pe.wait_ge(s_acc, b * ACC + MT + g + 1)
                if c == 0:
                    if h == 0 and m == MT - 1:
                        pe.wait_ge(s_acc, b * ACC + FREE + MT)
                    pe.wait_ge(s_tlo, b * 2 * MT + FREE + h * MT + m + 1)
                cols = slice(c * P, (c + 1) * P)
                for v, p in ((vt_hi, pt_hi), (vt_hi, pt_lo), (vt_lo, pt_hi)):
                    mm = nc.tensor.matmul(acc_ps[:, g % 2, :], v[:, m, cols], p[:, m, :],
                                          start=(m == 0 and v is vt_hi and p is pt_hi),
                                          stop=(m == MT - 1 and v is vt_lo))
                if m == MT - 1:
                    mm.then_inc(s_o, 1)

            def q_next(b):
                pe.wait_ge(s_exp, b * ST - 1)
                pe.wait_ge(s_x1lo_e, b * 2 + 2)
                pe.wait_ge(s_x1lo_o, b * 2 + 2)
                for k in range(KT):
                    mm = project_tile(wq_s, xs_hi, xs_lo, 0, k)
                mm.then_inc(s_q, 1)

            def k_next(b):
                pe.wait_ge(s_exp, b * ST)
                pe.wait_ge(s_x2lo, b * KT + KT)
                for k in range(KT):
                    mm = project_tile(wk_s, xs_hi, xs_lo, 1, k)
                mm.then_inc(s_k, 1)

            def batch(b, last):
                nb = b + 1
                for c in range(CT):
                    for m in range(MT):
                        if c < 2 and m % 4 == 0:
                            scores_here(b, NT + 2 * c + m // 4)
                        if c == 2 and m == 0 and not last:
                            q_next(nb)
                        out_part(b, 0, c, m)
                        if c == 0 and m < MT - VT:
                            turn(b, 0, VT + m)
                        if c == CT - 1:
                            turn(b, 1, m)
                for c in range(CT):
                    for m in range(MT):
                        if not last:
                            if c == 1 and m == 0:
                                k_next(nb)
                            if (c, m) in ((2, 4), (3, 0), (3, 4)):
                                scores_next(nb, 2 * c + m // 4 - 5)
                        out_part(b, 1, c, m)
                if last:
                    return
                scores_next(nb, 3)
                for m in range(MT):
                    v_group(nb, m)
                    if m >= MT - VT:
                        turn(nb, 0, m - (MT - VT))

            pe.wait_ge(s_id, 1)
            pe.wait_ge(s_wklo, 1)
            pe.wait_ge(s_acc, FREE)
            for k in range(KT):
                pe.wait_ge(s_x2lo, k + 1)
                mk = project_tile(wk_s, xs_hi, xs_lo, 1, k)
                if k == KT - 1:
                    mk.then_inc(s_k, 1)
                pe.wait_ge(s_wvlo, k + 1)
                for m in range(2):
                    mv = v_tile(m, k)
                    if k == KT - 1:
                        mv.then_inc(s_v, 1)
            v_group(0, 2)
            pe.wait_ge(s_wqlo, 1)
            for k in range(KT):
                pe.wait_ge((s_x1lo_e, s_x1lo_o)[k % 2], k // 2 + 1)
                mq = project_tile(wq_s, x0_hi, x0_lo, 0, k)
            mq.then_inc(s_q, 1)
            v_group(0, 3)
            v_group(0, 4)
            scores_next(0, 0)
            scores_next(0, 1)
            v_group(0, 5)
            scores_next(0, 2)
            scores_next(0, 3)
            v_group(0, 6)
            v_group(0, 7)
            for m in range(VT):
                turn(0, 0, m)
            with pe.Fori(0, B - 1) as b:
                batch(b, False)
            batch(B - 1, True)


_INS = ["x", "ctx_2048", "L0_xattn_Wq", "L0_xattn_bq", "L0_xattn_Wk", "L0_xattn_bk", "L0_xattn_Wv", "L0_xattn_bv"]


def kernel(**inputs):
    import numpy as _np
    import concourse.bacc as _bacc
    from concourse import mybir as _mybir
    from concourse.bass_utils import run_bass_kernel_spmd as _run

    nc = _bacc.Bacc("TRN2", target_bir_lowering=False, num_devices=1)
    arrays, args = {}, []
    for name in _INS:
        a = _np.asarray(inputs[name])
        if a.ndim == 2:
            a = a.T
        if name == "L0_xattn_bv":
            a = a.reshape(CT, P).T.reshape(C)
        a = _np.ascontiguousarray(a)
        arrays[f"in_{name}_dram"] = a
        args.append(nc.dram_tensor(f"in_{name}_dram", a.shape, _mybir.dt.from_np(a.dtype), kind="ExternalInput").ap())
    out = nc.dram_tensor("out_dram", (B, C, N), F32, kind="ExternalOutput").ap()
    build(nc, *args, out)
    r = _run(nc, [arrays], core_ids=[0])
    return r.results[0]["out_dram"]
```

```python
from contextlib import ExitStack

import concourse.bass as bass
from concourse import mybir

F32 = mybir.dt.float32
F32R = mybir.dt.float32r
ACT = mybir.ActivationFunctionType
ALU = mybir.AluOpType
AX_X = mybir.AxisListType.X

B, C, N, D = 8, 512, 1024, 64
P = 128
KT = C // P
CT = C // P
MT = N // P
HALVES = 2
NH = N // HALVES
NT = NH // P
ST = HALVES * NT
OG = HALVES * CT
ACC = MT + OG
BANKS = 4
OUTS = 4
Q = 32
NQ = P // Q
PAIRS = MT // 2
DVE_PAIRS = PAIRS // 2 + PAIRS
MOVED = NQ * NQ * 16


def build(nc, x1_d, x2_d, wq_d, bq_d, wk_d, bk_d, wv_d, bv_d, out_d):
    with ExitStack() as ctx:
        def sb(name, shape, dt):
            return ctx.enter_context(nc.sbuf_tensor(name, shape, dt))

        def psum(name, shape):
            return ctx.enter_context(nc.psum_tensor(name, shape, F32))

        def sem(name):
            return ctx.enter_context(nc.semaphore(name))

        stage = sb("stage", [P, KT, N], F32)
        xs_hi = sb("xs_hi", [P, KT, N], F32R)
        xs_lo = sb("xs_lo", [P, KT, N], F32R)
        vt_hi = sb("vt_hi", [P, MT, C], F32R)
        vt_lo = sb("vt_lo", [P, MT, C], F32R)
        probs = sb("probs", [P, 2, N], F32)
        blocks = sb("blocks", [P, N // Q, NT, Q], F32)
        pt_raw = sb("pt_raw", [P, MT, NH], F32)
        pt_hi = sb("pt_hi", [P, MT, NH], F32R)
        pt_lo = sb("pt_lo", [P, MT, NH], F32R)
        q_st = sb("q_st", [P, N], F32R)
        k_hh = sb("k_hh", [P, N], F32R)
        k_ll = sb("k_ll", [P, N], F32R)
        cross = sb("cross", [D, N], F32)
        full = sb("full", [D, N], F32)
        o_sb = sb("o_sb", [P, OUTS, NH], F32)
        wv_hi = sb("wv_hi", [P, KT, C], F32R)
        wv_lo = sb("wv_lo", [P, KT, C], F32R)
        wq_s = sb("wq_s", [P, KT, P], F32R)
        wk_s = sb("wk_s", [P, KT, P], F32R)
        ident = sb("ident", [P, P], F32)
        bias_q = sb("bias_q", [D, 1], F32)
        bias_k = sb("bias_k", [D, 1], F32)
        bias_v = sb("bias_v", [P, CT], F32)
        negmax = sb("negmax", [P, ST], F32)
        rowsum = sb("rowsum", [P, ST], F32)
        inv = sb("inv", [P, ST], F32)
        wv_raw = pt_raw[:, 0:KT, :]
        wq_raw = pt_raw[:, KT, 0:KT * D].rearrange("p (k d) -> p k d", d=D)
        wk_raw = pt_raw[:, KT, KT * D:2 * KT * D].rearrange("p (k d) -> p k d", d=D)
        x0_raw = blocks[:].rearrange("p (k a) t r -> p k (a t r)", k=KT)
        x0_hi = pt_hi[:].rearrange("p (k a) n -> p k (a n)", k=KT)
        x0_lo = pt_lo[:].rearrange("p (k a) n -> p k (a n)", k=KT)

        acc_ps = psum("acc_ps", [P, BANKS, NH])
        s_ps = psum("s_ps", [P, 2, 2, NH])

        s_wk = sem("s_wk")
        s_wq = sem("s_wq")
        s_bk = sem("s_bk")
        s_bqv = sem("s_bqv")
        s_wv = [sem(f"s_wv_{k}") for k in range(KT)]
        s_x0 = [sem(f"s_x0_{k}") for k in range(KT)]
        s_in = [sem(f"s_in_{k}") for k in range(KT)]
        s_res = [sem(f"s_res_{i}") for i in range(OUTS)]
        s_out = [sem(f"s_out_{i}") for i in range(OUTS)]
        s_moved = sem("s_moved")
        s_zero = sem("s_zero")
        s_ident = sem("s_ident")
        s_wkhi = sem("s_wkhi")
        s_wklo = sem("s_wklo")
        s_wqhi = sem("s_wqhi")
        s_wqlo = sem("s_wqlo")
        s_wvhi = sem("s_wvhi")
        s_wvlo = sem("s_wvlo")
        s_x1hi = sem("s_x1hi")
        s_x1lo_e = sem("s_x1lo_e")
        s_x1lo_o = sem("s_x1lo_o")
        s_x2hi = sem("s_x2hi")
        s_x2lo = sem("s_x2lo")
        s_x2lo_last = sem("s_x2lo_last")
        s_q = sem("s_q")
        s_k = sem("s_k")
        s_qcross = sem("s_qcross")
        s_kcross = sem("s_kcross")
        s_qsum = sem("s_qsum")
        s_ksum = sem("s_ksum")
        s_qhi = sem("s_qhi")
        s_qlo = sem("s_qlo")
        s_khi = sem("s_khi")
        s_klo = sem("s_klo")
        s_s = sem("s_s")
        s_max = sem("s_max")
        s_exp = sem("s_exp")
        s_inv = sem("s_inv")
        s_norm = sem("s_norm")
        s_blk = sem("s_blk")
        s_phi = sem("s_phi")
        s_plo = sem("s_plo")
        s_plo_odd = sem("s_plo_odd")
        s_used = sem("s_used")
        s_v = sem("s_v")
        s_vhi = sem("s_vhi")
        s_o = sem("s_o")
        s_acc = sem("s_acc")

        block = ctx.enter_context(nc.Block())

        def turned(t):
            return s_ps[:, t % 2, :, :].rearrange("p a (m r) -> p (a m) r", r=Q)

        def pt_tile(pt, t):
            return pt.rearrange("p m (i t r) -> p t (m i) r", i=NQ, t=NT)[:, t, :, :]

        def half_of(b, h):
            return b * HALVES + h

        @block.sync
        def _(sp):
            def load(src, b, k):
                sp.dma_start(stage[:, k, :], src[b, k * P:(k + 1) * P, :]).then_inc(s_in[k], 16)

            def residual(b, h, c):
                sp.dma_start(o_sb[:, c, :],
                             x1_d[b, c * P:(c + 1) * P, h * NH:(h + 1) * NH]).then_inc(s_res[c], 16)

            def next_residual(b, h, c):
                sp.wait_ge(s_out[c], half_of(b, h) * 16)
                residual(b, h, c)

            def store(b, h, c):
                sp.wait_ge(s_acc, b * ACC + BANKS + MT + h * CT + c + 1)
                sp.dma_start(out_d[b, c * P:(c + 1) * P, h * NH:(h + 1) * NH],
                             o_sb[:, c, :]).then_inc(s_out[c], 16)

            def move(b, h, steps=range(NQ)):
                if 0 in steps:
                    sp.wait_ge(s_blk, half_of(b, h) * NT + NT)
                for step in steps:
                    for i in range(NQ):
                        j = (i + step) % NQ
                        src = blocks[i * Q:(i + 1) * Q, :, :, :].rearrange("p (m j) t r -> p j m (t r)", j=NQ)
                        sp.dma_start(pt_raw[j * Q:(j + 1) * Q, :, i * P:(i + 1) * P],
                                     src[:, j, :, :]).then_inc(s_moved, 16)

            def next_x2(b, k):
                sp.wait_ge((s_x1lo_e, s_x1lo_o)[k % 2], b * 2 + k // 2 + 1)
                load(x2_d, b, k)

            def batch(b, last):
                nb = b + 1
                if not last:
                    for k in range(KT - 1):
                        sp.wait_ge(s_x2lo, b * (KT - 1) + k + 1)
                        load(x1_d, nb, k)
                    sp.wait_ge(s_x2lo_last, b + 1)
                    load(x1_d, nb, KT - 1)
                move(b, 1, range(0, 2))
                if not last:
                    next_x2(nb, 0)
                move(b, 1, range(2, NQ))
                if not last:
                    for k in range(1, KT):
                        next_x2(nb, k)
                store(b, 0, 0)
                store(b, 0, 1)
                next_residual(b, 1, 0)
                for c in (2, 3):
                    store(b, 0, c)
                    next_residual(b, 1, c - 1)
                store(b, 1, 0)
                next_residual(b, 1, 3)
                for c in range(1, CT):
                    store(b, 1, c)
                    if not last:
                        next_residual(nb, 0, c - 1)
                if not last:
                    move(nb, 0)
                    next_residual(nb, 0, CT - 1)

            for k in range(KT):
                load(x2_d, 0, k)
                if k == 0:
                    sp.dma_start(wk_raw, wk_d.rearrange("(k p) d -> p k d", p=P)).then_inc(s_wk, 16)
            for k in range(KT):
                sp.dma_start(wv_raw[:, k, :], wv_d[k * P:(k + 1) * P, :]).then_inc(s_wv[k], 16)
            sp.dma_start(wq_raw, wq_d.rearrange("(k p) d -> p k d", p=P)).then_inc(s_wq, 16)
            for k in range(KT):
                sp.dma_start(x0_raw[:, k, :], x1_d[0, k * P:(k + 1) * P, :]).then_inc(s_x0[k], 16)
                if k == 0:
                    sp.dma_start(bias_k[:], bk_d.rearrange("(d a) -> d a", a=1)).then_inc(s_bk, 16)
            sp.dma_start(bias_q[:], bq_d.rearrange("(d a) -> d a", a=1)).then_inc(s_bqv, 16)
            sp.dma_start(bias_v[:], bv_d.rearrange("(p c) -> p c", p=P)).then_inc(s_bqv, 16)
            for c in range(CT):
                residual(0, 0, c)
            with sp.Fori(0, B - 1) as b:
                batch(b, False)
            batch(B - 1, True)
            for i in range(OUTS):
                sp.wait_ge(s_out[i], 16 * B * HALVES)

        @block.gpsimd
        def _(pool):
            def low(out, src, hi):
                return nc.gpsimd.tensor_tensor(out, src, hi.bitcast(F32), ALU.subtract)

            nc.gpsimd.memset(ident[:], 0.0).then_inc(s_zero, 1)
            pool.wait_ge(s_zero, 1)
            nc.gpsimd.affine_select(out=ident[:], in_=ident[:], compare_op=ALU.not_equal, fill=1.0, base=0,
                                    pattern=[[-1, P]], channel_multiplier=1).then_inc(s_ident, 1)
            pool.wait_ge(s_wqhi, 1)
            low(wq_s[:, :, D:2 * D], wq_raw, wq_s[:, :, 0:D]).then_inc(s_wqlo, 1)
            for k in (0, 2):
                pool.wait_ge(s_x1hi, k + 1)
                low(x0_lo[:, k, :], x0_raw[:, k, :], x0_hi[:, k, :]).then_inc(s_x1lo_e, 1)
            def p_lo(b, j):
                pool.wait_ge(s_phi, half_of(b, 0) * PAIRS + j + 1)
                low(pt_lo[:, 2 * j:2 * j + 2, :], pt_raw[:, 2 * j:2 * j + 2, :],
                    pt_hi[:, 2 * j:2 * j + 2, :]).then_inc(s_plo_odd, 1)

            with pool.Fori(0, B - 1) as b:
                for k in (0, 2):
                    pool.wait_ge(s_x1hi, b * KT + KT + k + 1)
                    low(xs_lo[:, k, :], stage[:, k, :], xs_hi[:, k, :]).then_inc(s_x1lo_e, 1)
                for k in range(KT - 1):
                    pool.wait_ge(s_x2hi, b * KT + KT + k + 1)
                    low(xs_lo[:, k, :], stage[:, k, :], xs_hi[:, k, :]).then_inc(s_x2lo, 1)
                p_lo(b + 1, 1)
                p_lo(b + 1, 3)

        @block.scalar
        def _(act):
            def copy(out, in_):
                return nc.scalar.activation(out, in_, ACT.Copy)

            def round_x1(b, k):
                act.wait_ge(s_in[k], b * 32)
                copy(xs_hi[:, k, :], stage[:, k, :]).then_inc(s_x1hi, 1)

            def round_x2(b, k):
                act.wait_ge(s_in[k], b * 32 + 16)
                copy(xs_hi[:, k, :], stage[:, k, :]).then_inc(s_x2hi, 1)

            def cross_rows(slot):
                return copy(cross[:], s_ps[D:2 * D, slot, :, :].rearrange("p a n -> p (a n)"))

            def q_cross(b):
                act.wait_ge(s_q, b + 1)
                cross_rows(0).then_inc(s_qcross, 1)

            def q_high(b):
                act.wait_ge(s_qsum, b + 1)
                copy(q_st[0:D, :], full[:]).then_inc(s_qhi, 1)

            def k_cross(b):
                act.wait_ge(s_k, b + 1)
                cross_rows(1).then_inc(s_kcross, 1)

            def k_high(b):
                act.wait_ge(s_ksum, b + 1)
                for half in range(2):
                    copy(k_hh[half * D:(half + 1) * D, :], full[:]).then_inc(s_khi, 1)

            def exp(b, t, first=False):
                act.wait_ge(s_max, b * ST + t + 1)
                if not first:
                    act.wait_ge(s_blk, b * ST + t - 1)
                nc.scalar.activation(probs[:, t % 2, :], s_ps[:, t % 2, :, :].rearrange("p a n -> p (a n)"),
                                     ACT.Exp, bias=negmax[:, t:t + 1],
                                     accum_out=rowsum[:, t:t + 1]).then_inc(s_exp, 1)

            def v_hi(b, m):
                act.wait_ge(s_v, b * MT + m + 1)
                copy(vt_hi[:, m, :], acc_ps[:, m % BANKS, :]).then_inc(s_vhi, 1)

            def p_hi(b, h, j):
                if j == 0:
                    act.wait_ge(s_moved, half_of(b, h) * MOVED)
                if j < PAIRS - 1:
                    act.wait_ge(s_used, half_of(b, h) * (PAIRS - 1) - (PAIRS - 1) + j + 1)
                else:
                    act.wait_ge(s_o, half_of(b, h) * CT)
                copy(pt_hi[:, 2 * j:2 * j + 2, :], pt_raw[:, 2 * j:2 * j + 2, :]).then_inc(s_phi, 1)

            def v_phase(b):
                v_hi(b, 1)
                exp(b, 4)
                v_hi(b, 2)
                exp(b, 5)
                v_hi(b, 3)
                p_hi(b, 0, 0)
                p_hi(b, 0, 1)
                v_hi(b, 4)
                p_hi(b, 0, 2)
                p_hi(b, 0, 3)
                v_hi(b, 5)
                exp(b, 6)
                v_hi(b, 6)
                v_hi(b, 7)

            def batch(b, last):
                nb = b + 1
                if not last:
                    round_x1(nb, 0)
                    round_x1(nb, 1)
                exp(b, 7)
                if not last:
                    round_x1(nb, 2)
                    round_x1(nb, 3)
                    q_cross(nb)
                    round_x2(nb, 0)
                    q_high(nb)
                p_hi(b, 1, 0)
                if not last:
                    round_x2(nb, 1)
                p_hi(b, 1, 1)
                if not last:
                    round_x2(nb, 2)
                p_hi(b, 1, 2)
                p_hi(b, 1, 3)
                if not last:
                    round_x2(nb, 3)
                if last:
                    return
                k_cross(nb)
                k_high(nb)
                for t in range(NT):
                    exp(nb, t)
                v_hi(nb, 0)
                v_phase(nb)

            def first_p_hi(t):
                act.wait_ge(s_blk, t + 1)
                copy(pt_tile(pt_hi, t), turned(t)).then_inc(s_phi, 1)

            for k in range(KT):
                act.wait_ge(s_in[k], 16)
                copy(xs_hi[:, k, :], stage[:, k, :]).then_inc(s_x2hi, 1)
                if k == 0:
                    act.wait_ge(s_wk, 16)
                    copy(wk_s[:, :, 0:D], wk_raw).then_inc(s_wkhi, 1)
            for k in range(KT):
                act.wait_ge(s_wv[k], 16)
                copy(wv_hi[:, k, :], wv_raw[:, k, :]).then_inc(s_wvhi, 1)
            k_cross(0)
            act.wait_ge(s_wq, 16)
            copy(wq_s[:, :, 0:D], wq_raw).then_inc(s_wqhi, 1)
            for k in range(KT):
                if k == KT - 1:
                    v_hi(0, 0)
                act.wait_ge(s_x0[k], 16)
                copy(x0_hi[:, k, :], x0_raw[:, k, :]).then_inc(s_x1hi, 1)
            v_hi(0, 1)
            k_high(0)
            q_cross(0)
            v_hi(0, 2)
            q_high(0)
            v_hi(0, 3)
            exp(0, 0, first=True)
            exp(0, 1, first=True)
            v_hi(0, 4)
            first_p_hi(0)
            first_p_hi(1)
            v_hi(0, 5)
            exp(0, 2)
            exp(0, 3)
            v_hi(0, 6)
            first_p_hi(2)
            first_p_hi(3)
            exp(0, 4)
            v_hi(0, 7)
            exp(0, 5)
            exp(0, 6)
            with act.Fori(0, B - 1) as b:
                batch(b, False)
            batch(B - 1, True)

        @block.vector
        def _(dve):
            def sub(out, a, hi):
                return nc.vector.tensor_tensor(out, a, hi.bitcast(F32), ALU.subtract)

            def join(bias, slot):
                return nc.vector.scalar_tensor_tensor(
                    out=full[:], in0=s_ps[0:D, slot, :, :].rearrange("p a n -> p (a n)"), scalar=bias[:, 0:1],
                    in1=cross[:], op0=ALU.add, op1=ALU.add)

            def q_sum(b):
                dve.wait_ge(s_qcross, b + 1)
                join(bias_q, 0).then_inc(s_qsum, 1)

            def q_low(b):
                dve.wait_ge(s_qhi, b + 1)
                sub(q_st[D:2 * D, :], full[:], q_st[0:D, :]).then_inc(s_qlo, 1)

            def k_sum(b):
                dve.wait_ge(s_kcross, b + 1)
                join(bias_k, 1).then_inc(s_ksum, 1)

            def k_low(b):
                for half in range(2):
                    dve.wait_ge(s_khi, b * 2 + half + 1)
                    sub(k_ll[half * D:(half + 1) * D, :], full[:], k_hh[0:D, :]).then_inc(s_klo, 1)

            def low_x1(b, k):
                dve.wait_ge(s_x1hi, b * KT + k + 1)
                sub(xs_lo[:, k, :], stage[:, k, :], xs_hi[:, k, :]).then_inc(s_x1lo_o, 1)

            def low_x2(b, k):
                dve.wait_ge(s_x2hi, b * KT + k + 1)
                return sub(xs_lo[:, k, :], stage[:, k, :], xs_hi[:, k, :])

            def neg_max(b, t):
                dve.wait_ge(s_s, b * ST + t + 1)
                nc.vector.tensor_reduce(negmax[:, t:t + 1], s_ps[:, t % 2, :, :].rearrange("p a n -> p (a n)"),
                                        AX_X, ALU.max, negate=True).then_inc(s_max, 1)

            def normalise(b, t):
                dve.wait_ge(s_exp, b * ST + t + 1)
                nc.vector.reciprocal(inv[:, t:t + 1], rowsum[:, t:t + 1]).then_inc(s_inv, 1)
                dve.wait_ge(s_inv, b * ST + t + 1)
                nc.vector.tensor_scalar(probs[:, t % 2, :], probs[:, t % 2, :], inv[:, t:t + 1], None,
                                        ALU.mult).then_inc(s_norm, 1)

            def turn(b, t, first=False):
                h, i = t // NT, t % NT
                if i == 0 and not first:
                    dve.wait_ge(s_moved, half_of(b, h) * MOVED - MOVED)
                dve.wait_ge(s_norm, b * ST + t + 1)
                nc.vector.transpose(blocks[:, :, i, :],
                                    probs[:, t % 2, :].rearrange("p (j r) -> p j r", r=Q)).then_inc(s_blk, 1)

            def v_lo(b, m):
                dve.wait_ge(s_vhi, b * MT + m + 1)
                sub(vt_lo[:, m, :], acc_ps[:, m % BANKS, :], vt_hi[:, m, :]).then_inc(s_acc, 1)

            def p_lo(b, h, j):
                dve.wait_ge(s_phi, half_of(b, h) * PAIRS + j + 1)
                sub(pt_lo[:, 2 * j:2 * j + 2, :], pt_raw[:, 2 * j:2 * j + 2, :],
                    pt_hi[:, 2 * j:2 * j + 2, :]).then_inc(s_plo, 1)

            def out(b, h, c):
                dve.wait_ge(s_o, b * OG + h * CT + c + 1)
                dve.wait_ge(s_res[c], half_of(b, h) * 16 + 16)
                nc.vector.scalar_tensor_tensor(
                    out=o_sb[:, c, :], in0=acc_ps[:, c % BANKS, :], scalar=bias_v[:, c:c + 1],
                    in1=o_sb[:, c, :], op0=ALU.add, op1=ALU.add).then_inc(s_acc, 1)

            def v_phase(b):
                v_lo(b, 1)
                neg_max(b, 4)
                v_lo(b, 2)
                normalise(b, 4)
                neg_max(b, 5)
                v_lo(b, 3)
                normalise(b, 5)
                turn(b, 4)
                p_lo(b, 0, 0)
                v_lo(b, 4)
                neg_max(b, 6)
                p_lo(b, 0, 2)
                turn(b, 5)
                v_lo(b, 5)
                normalise(b, 6)
                v_lo(b, 6)
                neg_max(b, 7)
                turn(b, 6)
                v_lo(b, 7)
                normalise(b, 7)

            def batch(b, last):
                nb = b + 1
                dve.wait_ge(s_plo_odd, b * 2 + 2)
                turn(b, 7)
                if not last:
                    low_x1(nb, 1)
                    low_x1(nb, 3)
                out(b, 0, 0)
                out(b, 0, 1)
                if not last:
                    dve.wait_ge(s_klo, nb * 2)
                    q_sum(nb)
                    q_low(nb)
                out(b, 0, 2)
                for j in range(PAIRS - 1):
                    p_lo(b, 1, j)
                p_lo(b, 1, PAIRS - 1)
                if not last:
                    low_x2(nb, KT - 1).then_inc(s_x2lo_last, 1)
                out(b, 0, 3)
                out(b, 1, 0)
                if not last:
                    dve.wait_ge(s_qlo, nb + 1)
                    k_sum(nb)
                    k_low(nb)
                out(b, 1, 1)
                if last:
                    out(b, 1, 2)
                    out(b, 1, 3)
                    return
                neg_max(nb, 0)
                normalise(nb, 0)
                neg_max(nb, 1)
                turn(nb, 0)
                out(b, 1, 2)
                normalise(nb, 1)
                neg_max(nb, 2)
                turn(nb, 1)
                normalise(nb, 2)
                neg_max(nb, 3)
                turn(nb, 2)
                out(b, 1, 3)
                normalise(nb, 3)
                turn(nb, 3)
                v_lo(nb, 0)
                v_phase(nb)

            def first_p_lo(t):
                dve.wait_ge(s_phi, t + 1)
                sub(pt_tile(pt_lo, t), turned(t), pt_tile(pt_hi, t)).then_inc((s_plo, s_plo_odd)[t % 2], 1)

            nc.vector.memset(negmax[:], 0.0).then_inc(s_acc, BANKS)
            for k in range(KT):
                low_x2(0, k).then_inc(s_x2lo if k < KT - 1 else s_x2lo_last, 1)
                if k == 0:
                    dve.wait_ge(s_wkhi, 1)
                    sub(wk_s[:, :, D:2 * D], wk_raw, wk_s[:, :, 0:D]).then_inc(s_wklo, 1)
            for k in range(KT):
                dve.wait_ge(s_wvhi, k + 1)
                sub(wv_lo[:, k, :], wv_raw[:, k, :], wv_hi[:, k, :]).then_inc(s_wvlo, 1)
            dve.wait_ge(s_bk, 16)
            k_sum(0)
            for k in (1, 3):
                dve.wait_ge(s_x1hi, k + 1)
                sub(x0_lo[:, k, :], x0_raw[:, k, :], x0_hi[:, k, :]).then_inc(s_x1lo_o, 1)
                v_lo(0, k // 2)
            k_low(0)
            dve.wait_ge(s_bqv, 2 * 16)
            dve.wait_ge(s_klo, 2)
            q_sum(0)
            v_lo(0, 2)
            q_low(0)
            v_lo(0, 3)
            neg_max(0, 0)
            neg_max(0, 1)
            normalise(0, 0)
            normalise(0, 1)
            v_lo(0, 4)
            first_p_lo(0)
            first_p_lo(1)
            v_lo(0, 5)
            neg_max(0, 2)
            neg_max(0, 3)
            normalise(0, 2)
            normalise(0, 3)
            v_lo(0, 6)
            first_p_lo(2)
            first_p_lo(3)
            neg_max(0, 4)
            neg_max(0, 5)
            normalise(0, 4)
            v_lo(0, 7)
            dve.wait_ge(s_x1lo_e, 2)
            turn(0, 4, first=True)
            normalise(0, 5)
            neg_max(0, 6)
            turn(0, 5)
            neg_max(0, 7)
            normalise(0, 6)
            turn(0, 6)
            normalise(0, 7)
            with dve.Fori(0, B - 1) as b:
                batch(b, False)
            batch(B - 1, True)

        @block.tensor
        def _(pe):
            def project_tile(weights, hi, lo, slot, k, by_rows=False):
                for part, x in enumerate((hi, lo)):
                    for h in range(HALVES):
                        cols = x[:, k, h * NH:(h + 1) * NH]
                        if by_rows:
                            cols = cols.rearrange("p (i t r) -> p t i r", i=NQ, t=NT)
                        mm = nc.tensor.matmul(s_ps[:, slot, h, :], weights[:, k, :], cols,
                                              start=(k == 0 and part == 0), stop=(k == KT - 1 and part == 1))
                return mm

            def scores(t):
                rows = q_st[:, t * P:(t + 1) * P]
                for h in range(HALVES):
                    cols = slice(h * NH, (h + 1) * NH)
                    nc.tensor.matmul(s_ps[:, t % 2, h, :], rows, k_hh[:, cols], start=True, stop=False)
                    mm = nc.tensor.matmul(s_ps[:, t % 2, h, :], rows, k_ll[:, cols], start=False, stop=True)
                mm.then_inc(s_s, 1)

            def scores_first(b, t):
                if t == 0:
                    pe.wait_ge(s_qsum, b + 1)
                    pe.wait_ge(s_qlo, b + 1)
                    pe.wait_ge(s_klo, b * 2 + 2)
                else:
                    pe.wait_ge(s_ksum, b + 1)
                scores(t)

            def scores_next(b, t):
                pe.wait_ge(s_exp, b * ST + t - 1)
                scores(t)

            def v_tile(m, k):
                cols = slice(m * P, (m + 1) * P)
                for x, w in ((xs_hi, wv_hi), (xs_hi, wv_lo), (xs_lo, wv_hi)):
                    mm = nc.tensor.matmul(acc_ps[:, m % BANKS, :], x[:, k, cols], w[:, k, :],
                                          start=(k == 0 and w is wv_hi and x is xs_hi),
                                          stop=(k == KT - 1 and x is xs_lo))
                return mm

            def v_group(b, m, part=None):
                if part != 1:
                    pe.wait_ge(s_acc, b * ACC + m + 1)
                for k in range(KT // 2 if part == 1 else 0, KT // 2 if part == 0 else KT):
                    mm = v_tile(m, k)
                if part != 0:
                    mm.then_inc(s_v, 1)

            def out_part(b, h, c, m):
                if m == 0:
                    pe.wait_ge(s_acc, b * ACC + MT + h * CT + c + 1)
                if c == 0:
                    if h == 0:
                        pe.wait_ge(s_acc, b * ACC + BANKS + m + 1)
                    if m % 2 == 0:
                        j = m // 2
                        if h == 1:
                            pe.wait_ge(s_plo, b * DVE_PAIRS + PAIRS // 2 + j + 1)
                        elif j % 2 == 0:
                            pe.wait_ge(s_plo, b * DVE_PAIRS + j // 2 + 1)
                        else:
                            pe.wait_ge(s_plo_odd, b * 2 + j // 2 + 1)
                cols = slice(c * P, (c + 1) * P)
                for v, p in ((vt_hi, pt_hi), (vt_hi, pt_lo), (vt_lo, pt_hi)):
                    mm = nc.tensor.matmul(acc_ps[:, c % BANKS, :], v[:, m, cols], p[:, m, :],
                                          start=(m == 0 and v is vt_hi and p is pt_hi),
                                          stop=(m == MT - 1 and v is vt_lo))
                if m == MT - 1:
                    mm.then_inc(s_o, 1)
                elif c == CT - 1 and m % 2:
                    mm.then_inc(s_used, 1)

            def q_next(b):
                pe.wait_ge(s_exp, b * ST - 1)
                for k in range(KT):
                    pe.wait_ge((s_x1lo_e, s_x1lo_o)[k % 2], b * 2 + k // 2 + 1)
                    mm = project_tile(wq_s, xs_hi, xs_lo, 0, k, by_rows=True)
                mm.then_inc(s_q, 1)

            def k_next(b):
                pe.wait_ge(s_exp, b * ST)
                for k in range(KT):
                    if k < KT - 1:
                        pe.wait_ge(s_x2lo, b * (KT - 1) + k + 1)
                    else:
                        pe.wait_ge(s_x2lo_last, b + 1)
                    mm = project_tile(wk_s, xs_hi, xs_lo, 1, k)
                mm.then_inc(s_k, 1)

            def v_phase(b):
                tile_after = {1: 4, 2: 5, 4: 6, 5: 7}
                for m in range(1, MT):
                    v_group(b, m)
                    if m in tile_after:
                        scores_next(b, tile_after[m])

            def batch(b, last):
                nb = b + 1
                for c in range(CT):
                    for m in range(MT):
                        if (c, m) == (2, 0) and not last:
                            q_next(nb)
                        out_part(b, 0, c, m)
                for c in range(CT):
                    for m in range(MT):
                        if not last:
                            if (c, m) == (1, 0):
                                k_next(nb)
                            if (c, m) == (2, 3):
                                scores_first(nb, 0)
                            if (c, m) == (2, 6):
                                scores_first(nb, 1)
                            if (c, m) == (3, 1):
                                scores_next(nb, 2)
                            if (c, m) == (3, 5):
                                scores_next(nb, 3)
                        out_part(b, 1, c, m)
                if last:
                    return
                v_group(nb, 0)
                v_phase(nb)

            def first_turn(t):
                pe.wait_ge(s_norm, t + 1)
                for m in range(MT):
                    mm = nc.tensor.transpose(s_ps[:, t % 2, m // NT, (m % NT) * P:(m % NT + 1) * P],
                                             probs[:, t % 2, m * P:(m + 1) * P], ident[:])
                mm.then_inc(s_blk, 1)

            def first_scores(t):
                pe.wait_ge((s_plo, s_plo_odd)[t % 2], t // 2)
                scores(t)

            pe.wait_ge(s_wklo, 1)
            for k in range(KT):
                if k < KT - 1:
                    pe.wait_ge(s_x2lo, k + 1)
                else:
                    pe.wait_ge(s_x2lo_last, 1)
                mk = project_tile(wk_s, xs_hi, xs_lo, 1, k)
            mk.then_inc(s_k, 1)
            pe.wait_ge(s_acc, 1)
            for k in range(KT):
                pe.wait_ge(s_wvlo, k + 1)
                mv = v_tile(0, k)
            mv.then_inc(s_v, 1)
            v_group(0, 1)
            pe.wait_ge(s_wqlo, 1)
            for k in range(KT):
                if k == 2:
                    v_group(0, 2, part=0)
                pe.wait_ge((s_x1lo_e, s_x1lo_o)[k % 2], k // 2 + 1)
                mq = project_tile(wq_s, x0_hi, x0_lo, 0, k, by_rows=True)
            mq.then_inc(s_q, 1)
            v_group(0, 2, part=1)
            v_group(0, 3)
            v_group(0, 4, part=0)
            scores_first(0, 0)
            scores_first(0, 1)
            v_group(0, 4, part=1)
            v_group(0, 5, part=0)
            pe.wait_ge(s_ident, 1)
            first_turn(0)
            first_turn(1)
            v_group(0, 5, part=1)
            first_scores(2)
            first_scores(3)
            v_group(0, 6)
            first_turn(2)
            first_turn(3)
            v_group(0, 7, part=0)
            first_scores(4)
            first_scores(5)
            v_group(0, 7, part=1)
            scores_next(0, 6)
            scores_next(0, 7)
            with pe.Fori(0, B - 1) as b:
                batch(b, False)
            batch(B - 1, True)


_INS = ["x", "ctx_2048", "L0_xattn_Wq", "L0_xattn_bq", "L0_xattn_Wk", "L0_xattn_bk", "L0_xattn_Wv", "L0_xattn_bv"]


def kernel(**inputs):
    import numpy as _np
    import concourse.bacc as _bacc
    from concourse import mybir as _mybir
    from concourse.bass_utils import run_bass_kernel_spmd as _run

    nc = _bacc.Bacc("TRN2", target_bir_lowering=False, num_devices=1)
    arrays, args = {}, []
    for name in _INS:
        a = _np.asarray(inputs[name])
        if a.ndim == 2:
            a = a.T
        if name == "L0_xattn_bv":
            a = a.reshape(CT, P).T.reshape(C)
        a = _np.ascontiguousarray(a)
        arrays[f"in_{name}_dram"] = a
        args.append(nc.dram_tensor(f"in_{name}_dram", a.shape, _mybir.dt.from_np(a.dtype), kind="ExternalInput").ap())
    out = nc.dram_tensor("out_dram", (B, C, N), F32, kind="ExternalOutput").ap()
    build(nc, *args, out)
    r = _run(nc, [arrays], core_ids=[0])
    return r.results[0]["out_dram"]
```
